# Optimizing a Trainium2 kernel written in Bass

```python
import numpy as np
import jax
import jax.numpy as jnp

def _softmax(x, axis=-1):
    return jax.nn.softmax(x, axis=axis)
def _gelu(x):
    return jax.nn.gelu(x, approximate=True)
def _silu(x):
    return jax.nn.silu(x)
def _sigmoid(x):
    return jax.nn.sigmoid(x)
def _layernorm(x, axis=-1, eps=1e-5):
    m = jnp.mean(x, axis=axis, keepdims=True)
    v = jnp.var(x, axis=axis, keepdims=True)
    return (x - m) / jnp.sqrt(v + eps)
def _scatter_add(tgt, idx, src, axis=0):
    return tgt.at[idx].add(src)
def _segment_sum(src, seg, n):
    return jax.ops.segment_sum(src, seg, n)

kernel_name = 'mk_conv_seq_d2_conv_nchw512_54bc01'

def setup_inputs(seed: int = 0):
    np.random.seed(seed)
    _w = jnp.asarray
    def _rec_inputs():
        import jax
        import jax.numpy as jnp
        _gk = jax.random.key(seed)
        x = -0.0002928 + 1 * jax.random.normal(jax.random.fold_in(_gk, 1), (8, 512, 32, 32), jnp.float32)
        return x
    x = _rec_inputs()
    def _L0_conv_setup():
        import jax, jax.numpy as jnp
        import numpy as np
        import math
        GROUPS = 32
        EPS = 1e-05
        N_HEADS = 8

        def group_norm(x, w, b):
            B, C, T = x.shape
            xg = x.reshape(B, GROUPS, C // GROUPS * T)
            mu = xg.mean(axis=-1, keepdims=True)
            var = xg.var(axis=-1, keepdims=True)
            xn = ((xg - mu) * jax.lax.rsqrt(var + EPS)).reshape(B, C, T)
            return xn * w[None, :, None] + b[None, :, None]
        key = jax.random.key(seed)
        ks = jax.random.split(key, 7)
        C = 512
        return {'x': jax.random.normal(ks[0], (8, C, 32, 32), dtype=jnp.float32), 'norm_w': jax.random.normal(ks[1], (C,), dtype=jnp.float32), 'norm_b': jax.random.normal(ks[2], (C,), dtype=jnp.float32), 'qkv_w': jax.random.normal(ks[3], (3 * C, C), dtype=jnp.float32) * 0.02, 'qkv_b': jax.random.normal(ks[4], (3 * C,), dtype=jnp.float32) * 0.02, 'proj_w': jax.random.normal(ks[5], (C, C), dtype=jnp.float32) * 0.02, 'proj_b': jax.random.normal(ks[6], (C,), dtype=jnp.float32) * 0.02}
    _L0_conv_all = _L0_conv_setup()
    _L0_conv_in = {k: v for k, v in _L0_conv_all.items() if k in ('norm_w', 'norm_b', 'qkv_w', 'qkv_b', 'proj_w', 'proj_b', )}
    del _L0_conv_all

    def _L1_conv_setup():
        import jax, jax.numpy as jnp
        import numpy as np
        N_GROUPS = 32
        N_HEADS = 8
        D_K = 64
        EPS = 1e-05

        def group_norm(x, w, b):
            B, C, H, W = x.shape
            g = N_GROUPS
            xg = x.reshape(B, g, C // g, H, W)
            mean = xg.mean(axis=(2, 3, 4), keepdims=True)
            var = xg.var(axis=(2, 3, 4), keepdims=True)
            xg = (xg - mean) / jnp.sqrt(var + EPS)
            x = xg.reshape(B, C, H, W)
            return x * w[None, :, None, None] + b[None, :, None, None]
        key = jax.random.key(seed)
        ks = jax.random.split(key, 4)
        B, C, H, W = (16, 512, 32, 32)
        d_in = C
        d_qkv = N_HEADS * D_K * 3
        d_out = N_HEADS * D_K
        x = jax.random.normal(ks[0], (B, C, H, W), dtype=jnp.float32)
        norm_w = jnp.ones((C,), dtype=jnp.float32)
        norm_b = jnp.zeros((C,), dtype=jnp.float32)
        proj_w = jax.random.normal(ks[1], (d_qkv, d_in), dtype=jnp.float32) * d_in ** (-0.5)
        proj_b = jnp.zeros((d_qkv,), dtype=jnp.float32)
        out_w = jax.random.normal(ks[2], (C, d_out), dtype=jnp.float32) * d_out ** (-0.5)
        out_b = jnp.zeros((C,), dtype=jnp.float32)
        return {'x': x, 'norm_w': norm_w, 'norm_b': norm_b, 'proj_w': proj_w, 'proj_b': proj_b, 'out_w': out_w, 'out_b': out_b}
    _L1_conv_all = _L1_conv_setup()
    _L1_conv_in = {k: v for k, v in _L1_conv_all.items() if k in ('norm_w', 'norm_b', 'proj_w', 'proj_b', 'out_w', 'out_b', )}
    del _L1_conv_all

    return {
        "x": x,
        "L0_conv_norm_w": _L0_conv_in["norm_w"],
        "L0_conv_norm_b": _L0_conv_in["norm_b"],
        "L0_conv_qkv_w": _L0_conv_in["qkv_w"],
        "L0_conv_qkv_b": _L0_conv_in["qkv_b"],
        "L0_conv_proj_w": _L0_conv_in["proj_w"],
        "L0_conv_proj_b": _L0_conv_in["proj_b"],
        "L1_conv_norm_w": _L1_conv_in["norm_w"],
        "L1_conv_norm_b": _L1_conv_in["norm_b"],
        "L1_conv_proj_w": _L1_conv_in["proj_w"],
        "L1_conv_proj_b": _L1_conv_in["proj_b"],
        "L1_conv_out_w": _L1_conv_in["out_w"],
        "L1_conv_out_b": _L1_conv_in["out_b"],
    }

def reference(x, L0_conv_norm_w, L0_conv_norm_b, L0_conv_qkv_w, L0_conv_qkv_b, L0_conv_proj_w, L0_conv_proj_b, L1_conv_norm_w, L1_conv_norm_b, L1_conv_proj_w, L1_conv_proj_b, L1_conv_out_w, L1_conv_out_b):
    import jax
    import jax.numpy as jnp
    def _L0_conv_ref(x, norm_w, norm_b, qkv_w, qkv_b, proj_w, proj_b):
        import jax, jax.numpy as jnp
        import numpy as np
        import math
        GROUPS = 32
        EPS = 1e-05
        N_HEADS = 8

        def group_norm(x, w, b):
            B, C, T = x.shape
            xg = x.reshape(B, GROUPS, C // GROUPS * T)
            mu = xg.mean(axis=-1, keepdims=True)
            var = xg.var(axis=-1, keepdims=True)
            xn = ((xg - mu) * jax.lax.rsqrt(var + EPS)).reshape(B, C, T)
            return xn * w[None, :, None] + b[None, :, None]
        b, c, H, W = x.shape
        T = H * W
        xf = x.reshape(b, c, T)
        xn = group_norm(xf, norm_w, norm_b)
        qkv = jnp.einsum('oc,bct->bot', qkv_w, xn) + qkv_b[None, :, None]
        ch = c // N_HEADS
        qkv = qkv.reshape(b * N_HEADS, 3 * ch, T)
        q, k, v = (qkv[:, :ch], qkv[:, ch:2 * ch], qkv[:, 2 * ch:])
        scale = 1.0 / math.sqrt(math.sqrt(ch))
        weight = jnp.einsum('bct,bcs->bts', q * scale, k * scale)
        weight = jax.nn.softmax(weight.astype(jnp.float32), axis=-1).astype(qkv.dtype)
        a = jnp.einsum('bts,bcs->bct', weight, v).reshape(b, c, T)
        hout = jnp.einsum('oc,bct->bot', proj_w, a) + proj_b[None, :, None]
        return (xf + hout).reshape(b, c, H, W)

    def _L1_conv_ref(x, norm_w, norm_b, proj_w, proj_b, out_w, out_b):
        import jax, jax.numpy as jnp
        import numpy as np
        N_GROUPS = 32
        N_HEADS = 8
        D_K = 64
        EPS = 1e-05

        def group_norm(x, w, b):
            B, C, H, W = x.shape
            g = N_GROUPS
            xg = x.reshape(B, g, C // g, H, W)
            mean = xg.mean(axis=(2, 3, 4), keepdims=True)
            var = xg.var(axis=(2, 3, 4), keepdims=True)
            xg = (xg - mean) / jnp.sqrt(var + EPS)
            x = xg.reshape(B, C, H, W)
            return x * w[None, :, None, None] + b[None, :, None, None]
        B, C, H, W = x.shape
        S = H * W
        scale = D_K ** (-0.5)
        h = group_norm(x, norm_w, norm_b)
        tokens = h.reshape(B, C, S).transpose(0, 2, 1)
        qkv = tokens @ proj_w.T + proj_b
        qkv = qkv.reshape(B, S, N_HEADS, 3 * D_K)
        q, k, v = jnp.split(qkv, 3, axis=-1)
        attn = jnp.einsum('bihd,bjhd->bijh', q, k) * scale
        attn = jax.nn.softmax(attn, axis=2)
        res = jnp.einsum('bijh,bjhd->bihd', attn, v)
        res = res.reshape(B, S, N_HEADS * D_K)
        res = res @ out_w.T + out_b
        res = res.transpose(0, 2, 1).reshape(B, C, H, W)
        return res + x

    def _gn(v, G=32, eps=1e-5):
        B_, C_, H_, W_ = v.shape
        g = v.reshape(B_, G, C_ // G, H_, W_)
        m = jnp.mean(g, axis=(2, 3, 4), keepdims=True)
        s = jnp.var(g, axis=(2, 3, 4), keepdims=True)
        return ((g - m) / jnp.sqrt(s + eps)).reshape(v.shape)

    def _ln_c(v, eps=1e-6):
        m = jnp.mean(v, axis=1, keepdims=True)
        s = jnp.var(v, axis=1, keepdims=True)
        return (v - m) / jnp.sqrt(s + eps)

    def _ln_t(v, eps=1e-5):
        m = jnp.mean(v, axis=-1, keepdims=True)
        s = jnp.var(v, axis=-1, keepdims=True)
        return (v - m) / jnp.sqrt(s + eps)

    def _to_tokens(v):
        B_, C_, H_, W_ = v.shape
        return v.reshape(B_, C_, H_ * W_).transpose(0, 2, 1)
    def _from_tokens(t, like):
        B_, C_, H_, W_ = like.shape
        return t.transpose(0, 2, 1).reshape(B_, C_, H_, W_)

    x = _L0_conv_ref(x, L0_conv_norm_w, L0_conv_norm_b, L0_conv_qkv_w, L0_conv_qkv_b, L0_conv_proj_w, L0_conv_proj_b)
    x = _L1_conv_ref(x, L1_conv_norm_w, L1_conv_norm_b, L1_conv_proj_w, L1_conv_proj_b, L1_conv_out_w, L1_conv_out_b)
    return x


_drawn_inputs = setup_inputs


def setup_inputs(seed=0):
    import zlib

    import numpy as np

    out = dict(_drawn_inputs(seed))
    spreads = {'L1_conv_norm_w': (1.0, 0.2),
     'L1_conv_norm_b': (0.0, 0.1),
     'L1_conv_proj_b': (0.0, 0.1),
     'L1_conv_out_b': (0.0, 0.1)}
    factors = {'L0_conv_norm_w': 5.56, 'L0_conv_qkv_b': 4.602, 'L0_conv_proj_b': 2.968}
    for name, (base, spread) in spreads.items():
        noise = np.random.default_rng([zlib.crc32(name.encode()), seed]).standard_normal(out[name].shape)
        drawn = base * np.exp(spread * noise) if base else spread * noise
        out[name] = jnp.asarray(drawn.astype(out[name].dtype))
    for name, factor in factors.items():
        out[name] = (out[name] * factor).astype(out[name].dtype)
    return out
```

```python
from contextlib import ExitStack

import numpy as np

import concourse.bass as bass
from concourse import mybir

F32 = mybir.dt.float32
F32R = mybir.dt.float32r
I32 = mybir.dt.int32
ALU = mybir.AluOpType
ACT = mybir.ActivationFunctionType
AX = mybir.AxisListType

P = 128
B = 8
LAYERS = 2
C = 512
T = 1024
H = 8
D = C // H
KT = C // P
HALF = 512
NT = T // P
TILES = H * NT
PASSES = LAYERS * B
GROUP = 2 * P
GROUPS = TILES // 2
BLK = T // P
PAIRS = H // 2
PT_STEPS = 2 * NT
NORM_GROUPS = 32
EPS = 1e-5
SCALE = 1.0 / np.sqrt(D)
RSQRT_SEED = 0x5F3759DF
LO_CREDIT, SUM_CREDIT, SPLIT_CREDIT, OUT_CREDIT, PV_CREDIT, STORE_CREDIT = 2, 1, 4, 8, 1, 1
CHAIN = 20
LATER_QK_N = [3] * 12 + [2, 2, 2, 6]
LATER_QK = [sum(LATER_QK_N[m // 4 * 4:m]) for m in range(PT_STEPS)]


def build(nc, x, wqk, wv, wp, bqk, bv, bo, nw, nb, consts, out):
    mid = nc.dram_tensor("layer0_out", (B, C, T), F32, kind="Internal").ap()

    with ExitStack() as ctx:
        base = [(nc.sbuf_base + 63) // 64 * 64]

        def sb(name, shape, dt, at=None):
            size = int(np.prod(shape[1:])) * 4
            where = base[0] if at is None else at
            t = nc.alloc_sbuf_tensor_at(name, shape, dt, offset=where)
            if at is None:
                base[0] += (size + 31) // 32 * 32
            return t

        def sem(name):
            return ctx.enter_context(nc.semaphore(name))

        def f32(ap):
            return ap.bitcast(F32)

        wp_hi = sb("wp_hi", [P, KT, C], F32R)
        wp_at = base[0]
        wp_lo = sb("wp_lo", [P, KT, C], F32R)
        wp_raw = sb("wp_raw", [P, KT, C], F32, at=wp_at)
        pt_hi = sb("pt_hi", [P, 2, BLK, GROUP], F32R)
        pt_lo = sb("pt_lo", [P, 2, BLK, GROUP], F32R)
        wv_raw = [sb(f"wv_raw{s}", [P, C], F32) for s in range(2)]
        wqk_hi = [sb(f"wqk_hi{s}", [P, KT, P], F32R) for s in range(2)]
        wqk_at = [base[0] + s * KT * P * 4 for s in range(2)]
        wqk_lo = [sb(f"wqk_lo{s}", [P, KT, P], F32R) for s in range(2)]
        wqk_raw = [sb(f"wqk_raw{s}", [P, KT, P], F32, at=wqk_at[s]) for s in range(2)]
        xn_hi = sb("xn_hi", [P, KT, T], F32R)
        x_at = base[0]
        xn_lo = sb("xn_lo", [P, KT, T], F32R)
        x_raw = sb("x_raw", [P, KT, T], F32, at=x_at)
        qk = sb("qk", [P, T], F32)
        q_st = [sb(f"q_st{s}", [P, T], F32R) for s in range(2)]
        kh_st = [sb(f"kh_st{s}", [P, T], F32R) for s in range(2)]
        kl_st = [sb(f"kl_st{s}", [P, T], F32R) for s in range(2)]
        v_raw = sb("v_raw", [P, BLK, C], F32)
        v_st = [sb(f"v_st{s}", [P, BLK, 2 * D], F32R) for s in range(2)]
        attn = sb("attn", [P, T], F32)
        o_part = [sb(f"o_part{s}", [P, GROUP], F32) for s in range(2)]
        a_hi = sb("a_hi", [P, PAIRS, T], F32R)
        a_lo = sb("a_lo", [P, PAIRS, T], F32R)
        probs = [sb(f"probs{s}", [P, T], F32) for s in range(2)]
        stage = probs + [sb(f"stage{s}", [P, T], F32) for s in range(2)]
        bv_all = sb("bv_all", [P, LAYERS, C], F32)
        const_sb = sb("const_sb", [P, 2 * P], F32)
        ident, group_mean = const_sb[:, 0:P], const_sb[:, P:2 * P]
        bqk_sb = sb("bqk_sb", [P, LAYERS * H], F32)
        bqk_sc = sb("bqk_sc", [P, LAYERS * H], F32)
        bo_sb = sb("bo_sb", [P, LAYERS * KT], F32)
        nw_sb = sb("nw_sb", [P, LAYERS * KT], F32)
        nb_sb = sb("nb_sb", [P, LAYERS * KT], F32)
        qk_scale = sb("qk_scale", [P, 1], F32)
        row_min = sb("row_min", [P, 4], F32)
        row_sum = sb("row_sum", [P, 4], F32)
        row_rcp = sb("row_rcp", [P, 4], F32)
        bn_part = sb("bn_part", [P, KT, 12], F32)
        bn = sb("bn", [P, KT, 2], F32)
        gmean = sb("gmean", [P, KT], F32)
        work = sb("work", [P, KT], F32)
        spread = sb("spread", [P, KT], F32)
        var_eps = sb("var_eps", [P, KT], F32)
        neg_half = sb("neg_half", [P, KT], F32)
        seed = sb("seed", [P, KT], I32)
        rstd_bits = sb("rstd_bits", [P, KT], I32)
        rstd = rstd_bits[:, :].bitcast(F32)
        norm_a = sb("norm_a", [P, KT], F32)
        norm_b = sb("norm_b", [P, KT], F32)
        scratch = sb("scratch", [P, 8], F32)
        assert base[0] <= nc.sbuf_usable_end, (base[0], nc.sbuf_usable_end)

        wv_hi = pt_hi[:, :, :, :].rearrange("p a b c -> p (a b c)")[:, 0:KT * C].rearrange("p (k n) -> p k n", k=KT)
        wv_lo = pt_lo[:, :, :, :].rearrange("p a b c -> p (a b c)")[:, 0:KT * C].rearrange("p (k n) -> p k n", k=KT)

        ps_s = ctx.enter_context(nc.psum_tensor("ps_s", [P, 2, T], F32))
        ps_t = ctx.enter_context(nc.psum_tensor("ps_t", [P, 2, HALF], F32))
        ps_o = ctx.enter_context(nc.psum_tensor("ps_o", [P, HALF], F32))
        ps_g = ctx.enter_context(nc.psum_tensor("ps_g", [P, HALF], F32))
        s_bank = [ps_s[:, n // 2, (n % 2) * HALF:(n % 2 + 1) * HALF] for n in range(4)]
        t_bank = [ps_t[:, n, :] for n in range(2)]
        o_bank, g_bank = ps_o[:, :], ps_g[:, :]
        stat_bank = t_bank[1]
        out_bank = s_bank + t_bank + [g_bank, o_bank]
        qk_bank = {0: s_bank[0:2], 1: s_bank[2:4]}
        v_bank = 2 * (t_bank + [g_bank, o_bank])

        const_loaded = sem("const_loaded")
        x_loaded = [sem(f"x_loaded{c}") for c in range(KT)]
        wqk_loaded = [sem(f"wqk_loaded{s}") for s in range(2)]
        wp_loaded = sem("wp_loaded")
        wv_loaded = [sem(f"wv_loaded{s}") for s in range(2)]
        q_moved = sem("q_moved")
        stacked = [sem(f"stacked{s}") for s in range(2)]
        res_loaded = sem("res_loaded")
        res_loaded_p = sem("res_loaded_p")
        out_stored = sem("out_stored")
        wqk_hi_done = sem("wqk_hi_done")
        wqk_ready = sem("wqk_ready")
        wv_hi_done = sem("wv_hi_done")
        wv_ready = sem("wv_ready")
        wp_hi_done = sem("wp_hi_done")
        wp_ready = sem("wp_ready")
        xn_f32 = sem("xn_f32")
        xn_hi_done = sem("xn_hi_done")
        xn_ready = sem("xn_ready")
        qk_acc = sem("qk_acc")
        qk_evac = sem("qk_evac")
        qk_hi_done = sem("qk_hi_done")
        qk_split = sem("qk_split")
        v_acc = sem("v_acc")
        v_evac = sem("v_evac")
        v_hi_done = sem("v_hi_done")
        v_ready = sem("v_ready")
        scores_ready = sem("scores_ready")
        min_ready = sem("min_ready")
        exp_ready = sem("exp_ready")
        rcp_ready = sem("rcp_ready")
        probs_ready = sem("probs_ready")
        transposed = sem("transposed")
        hi_ready = sem("hi_ready")
        lo_ready = sem("lo_ready")
        pv_done = sem("pv_done")
        part_ready = sem("part_ready")
        attn_ready = sem("attn_ready")
        a_hi_done = sem("a_hi_done")
        a_ready = sem("a_ready")
        proj_acc = sem("proj_acc")
        out_ready = sem("out_ready")
        half_stat_ready = sem("half_stat_ready")
        stat_ready = sem("stat_ready")
        stat_sum = sem("stat_sum")
        chain = sem("chain")
        setup_done = sem("setup_done")
        waits_passed = sem("waits_passed")

        def within(value, low, high):
            return value.with_bounds(min_val=low, max_val=high)

        def next_pass(i):
            return within(i + 1 - (i + 1) // PASSES, 0, PASSES - 1)

        def lo_at(n, half):
            return 2 * n + half + 1 + LO_CREDIT

        def sum_at(g):
            return g + 1 + SUM_CREDIT

        def a_at(pair, k):
            return 4 * pair + k + 1 + SPLIT_CREDIT

        def pv_at(g):
            return g + 1 + PV_CREDIT

        def stored_before(i):
            return 64 * i + STORE_CREDIT

        def out_at(i, q):
            return 8 * i + q + 1 + OUT_CREDIT

        def wait_alone(eng, semaphore, value):
            eng.wait_ge(semaphore, value)
            eng.sem_inc(waits_passed, 1)

        block = ctx.enter_context(nc.Block())

        @block.sync
        def _(sp):
            def load_x(source, image):
                for c in range(KT):
                    sp.dma_start(x_raw[:, c, :], source[image, c * P:(c + 1) * P, :]).then_inc(x_loaded[c], 16)

            def load_wqk(row, s):
                sp.dma_start(wqk_raw[s][:, :, :], wqk[row, :, :, :]).then_inc(wqk_loaded[s], 16)

            def load_wv(layer, k):
                sp.dma_start(wv_raw[k % 2][:, :], wv[layer, k, :, :]).then_inc(wv_loaded[k % 2], 16)

            def load_wp(layer):
                sp.dma_start(wp_raw[:, :, :], wp[layer, :, :, :].rearrange("k p n -> p k n")).then_inc(wp_loaded, 16)

            def stack(hd, s):
                sp.wait_ge(qk_split, 2 * hd + 2)
                sp.dma_start(f32(q_st[s][0:D, :]), f32(kh_st[s][0:D, :])).then_inc(q_moved, 16)
                sp.dma_start(f32(q_st[s][D:P, :]), f32(kl_st[s][0:D, :])).then_inc(q_moved, 16)
                sp.wait_ge(q_moved, 32 * (hd + 1))
                sp.dma_start(f32(kh_st[s][0:D, :]), f32(kh_st[s][D:P, :])).then_inc(stacked[s], 16)
                sp.dma_start(f32(kl_st[s][0:D, :]), f32(kl_st[s][D:P, :])).then_inc(stacked[s], 16)

            def load_res(i, o, done):
                with sp.If(i < B):
                    sp.dma_start(stage[o][:, :], x[within(i, 0, B - 1), o * P:(o + 1) * P, :]).then_inc(done, 16)
                with sp.Else():
                    sp.dma_start(stage[o][:, :], mid[within(i - B, 0, B - 1), o * P:(o + 1) * P, :]).then_inc(done, 16)

            load_x(x, 0)
            sp.dma_start(const_sb[:, :], consts).then_inc(const_loaded, 16)
            sp.dma_start(bqk_sb[:, :], bqk).then_inc(const_loaded, 16)
            sp.dma_start(bo_sb[:, :], bo).then_inc(const_loaded, 16)
            sp.dma_start(nw_sb[:, :], nw).then_inc(const_loaded, 16)
            sp.dma_start(nb_sb[:, :], nb).then_inc(const_loaded, 16)
            sp.dma_start(bv_all[:, :, :], bv.rearrange("(o l) n -> o l n", o=1).broadcast_to([P, LAYERS, C])).then_inc(const_loaded, 16)
            load_wqk(0, 0)
            load_wqk(1, 1)
            for k in range(KT):
                if k >= 2:
                    sp.wait_ge(wv_ready, k - 1)
                load_wv(0, k)
            load_wp(0)

            with sp.Fori(0, PASSES) as i:
                layer = i // B
                nxt = within(i + 1 - (i + 1) // PASSES, 0, PASSES - 1)
                next_layer = within(nxt // B, 0, LAYERS - 1)
                hd0 = H * i
                sp.wait_ge(qk_acc, 2 * hd0 + 2)
                load_wqk(layer * H + 2, 0)
                stack(hd0, 0)
                with sp.Fori(0, PAIRS - 1) as p:
                    for e in range(2):
                        hh = 2 * p + e
                        wait_alone(sp, qk_acc, 2 * (hd0 + hh + 2))
                        if e == 0:
                            load_wqk(within(layer * H + hh + 3, 0, LAYERS * H - 1), 1)
                        else:
                            with sp.If(p < PAIRS - 2):
                                load_wqk(within(layer * H + hh + 3, 0, LAYERS * H - 1), 0)
                            with sp.Else():
                                load_wqk(next_layer * H, 0)
                        stack(hd0 + hh + 1, 1 - e)
                wait_alone(sp, qk_acc, 2 * (hd0 + H))
                with sp.If(nxt < B):
                    load_x(x, within(nxt, 0, B - 1))
                with sp.Else():
                    load_x(mid, within(nxt - B, 0, B - 1))
                load_wqk(next_layer * H + 1, 1)
                stack(hd0 + H - 1, 1)
                wait_alone(sp, out_stored, stored_before(i))
                load_res(i, 2, res_loaded)
                load_res(i, 3, res_loaded)
                for k in range(2):
                    sp.wait_ge(wv_ready, KT * i + k + 3)
                    load_wv(next_layer, k)
                wait_alone(sp, transposed, 2 * TILES * (i + 1))
                load_res(i, 0, res_loaded_p)
                load_res(i, 1, res_loaded_p)
                for k in range(2, KT):
                    sp.wait_ge(wv_ready, KT * (i + 1) + k - 1)
                    load_wv(next_layer, k)
                for o in range(KT):
                    wait_alone(sp, out_ready, out_at(i, 2 * o + 1))
                    with sp.If(i < B):
                        sp.dma_start(mid[within(i, 0, B - 1), o * P:(o + 1) * P, :], stage[o][:, :]).then_inc(out_stored, 16)
                    with sp.Else():
                        sp.dma_start(out[within(i - B, 0, B - 1), o * P:(o + 1) * P, :], stage[o][:, :]).then_inc(out_stored, 16)
                with sp.If(i < B):
                    with sp.If(i > B - 2):
                        load_wp(1)
            sp.wait_ge(out_stored, stored_before(PASSES))

        @block.gpsimd
        def _(pool):
            def split_wqk(hd, s, pair):
                wait_alone(pool, wqk_loaded[s], 16 * (pair + 1))
                nc.gpsimd.tensor_scalar(wqk_hi[s][:, :, :], wqk_raw[s][:, :, :], 1.0, 1.0, ALU.mult, ALU.mult).then_inc(wqk_hi_done, 1)
                pool.wait_ge(wqk_hi_done, hd + 1)
                nc.gpsimd.tensor_tensor(wqk_lo[s][:, :, :], wqk_raw[s][:, :, :], f32(wqk_hi[s][:, :, :]),
                                        ALU.subtract).then_inc(wqk_ready, 1)

            def split_wv(seq, k):
                wait_alone(pool, wv_loaded[k % 2], 16 * (2 * seq + k // 2 + 1))
                nc.gpsimd.tensor_scalar(wv_hi[:, k, :], wv_raw[k % 2][:, :], 1.0, 1.0, ALU.mult, ALU.mult).then_inc(wv_hi_done, 1)
                pool.wait_ge(wv_hi_done, KT * seq + k + 1)
                nc.gpsimd.tensor_tensor(wv_lo[:, k, :], wv_raw[k % 2][:, :], f32(wv_hi[:, k, :]),
                                        ALU.subtract).then_inc(wv_ready, 1)

            def split_wp(layer, k):
                wait_alone(pool, wp_loaded, 16 * (layer + 1))
                nc.gpsimd.tensor_scalar(wp_hi[:, k, :], wp_raw[:, k, :], 1.0, 1.0, ALU.mult, ALU.mult).then_inc(wp_hi_done, 1)
                pool.wait_ge(wp_hi_done, KT * layer + k + 1)
                nc.gpsimd.tensor_tensor(wp_lo[:, k, :], wp_raw[:, k, :], f32(wp_hi[:, k, :]),
                                        ALU.subtract).then_inc(wp_ready, 1)

            def split_qk(hd, s, half):
                cols = slice(half * HALF, (half + 1) * HALF)
                wait_alone(pool, qk_evac, 2 * hd + half + 1)
                nc.gpsimd.tensor_scalar(kh_st[s][:, cols], qk[:, cols], 1.0, 1.0, ALU.mult, ALU.mult).then_inc(qk_hi_done, 1)
                pool.wait_ge(qk_hi_done, 2 * hd + half + 1)
                nc.gpsimd.tensor_tensor(kl_st[s][:, cols], qk[:, cols], f32(kh_st[s][:, cols]),
                                        ALU.subtract).then_inc(qk_split, 1)

            def v_low(hd, hh, s):
                pool.wait_ge(v_hi_done, hd + 1)
                nc.gpsimd.tensor_tensor(v_st[s][:, :, D:2 * D], v_raw[:, :, bass.ds(hh * D, D)],
                                        f32(v_st[s][:, :, 0:D]), ALU.subtract).then_inc(v_ready, 1)

            def normalise(n, m):
                wait_alone(pool, rcp_ready, n + 1)
                nc.gpsimd.tensor_scalar(probs[m % 2][:, :], probs[m % 2][:, :], row_rcp[:, m % 4:m % 4 + 1], 1.0,
                                        ALU.mult, ALU.mult).then_inc(probs_ready, 1)

            def x_normalise(seq, c):
                if c == 0:
                    wait_alone(pool, chain, CHAIN * (seq + 1))
                nc.gpsimd.tensor_scalar(x_raw[:, c, :], x_raw[:, c, :], norm_a[:, c:c + 1], norm_b[:, c:c + 1],
                                        ALU.mult, ALU.add).then_inc(xn_f32, 1)

            nc.gpsimd.memset(scratch[:, 4:6], 0.0).then_inc(a_ready, SPLIT_CREDIT)
            nc.gpsimd.memset(scratch[:, 6:8], 0.0).then_inc(out_stored, STORE_CREDIT)
            split_wqk(0, 0, 0)
            for c in range(KT):
                x_normalise(0, c)
            for k in range(KT):
                split_wv(0, k)
            split_wqk(1, 1, 0)

            def attn_split(pair, p, k):
                cols = slice(k * GROUP, (k + 1) * GROUP)
                src = attn[:, cols].rearrange("p (o t) -> p o t", o=1)
                hi, lo = a_hi[:, bass.ds(p, 1), cols], a_lo[:, bass.ds(p, 1), cols]
                pool.wait_ge(attn_ready, sum_at(8 * pair + 4 + k))
                pool.wait_ge(a_hi_done, 4 * pair + k + 1)
                nc.gpsimd.tensor_tensor(lo, src, f32(hi), ALU.subtract).then_inc(a_ready, 1)

            def pair_steps(i, p, last):
                pair = PAIRS * i + p
                tile = TILES * i + PT_STEPS * p
                for e in range(2):
                    hh = 2 * p + e
                    hd = H * i + hh
                    for j in range(NT):
                        m = NT * e + j
                        if j == 1 and not (last and e == 1):
                            split_qk(hd + 1, 1 - e, 1)
                        if j == 3 and not (last and e == 1):
                            v_low(hd + 1, hh + 1, 1 - e)
                        if e == 1 and j in (5, 7):
                            attn_split(pair, p, (j - 5) // 2)
                        if j == 4 + e and not (last and e == 1):
                            split_wqk(hd + 3, 1 - e, pair + 1 + e)
                        if j == 6 and not last:
                            pool.wait_ge(scores_ready, tile + NT * (e + 1))
                            split_qk(hd + 2, e, 0)
                        if not (last and m + 2 >= PT_STEPS):
                            normalise(tile + m + 2, m + 2)
                attn_split(pair, p, 2)
                if last:
                    pool.wait_ge(pv_done, pv_at(8 * pair + 7))
                    split_wv(i + 1, 0)
                attn_split(pair, p, 3)
                if last:
                    split_wv(i + 1, 1)
                    for c in range(KT):
                        x_normalise(i + 1, c)
                    for k in range(2, KT):
                        split_wv(i + 1, k)

            with pool.Fori(0, PASSES) as i:
                hd0 = H * i
                split_qk(hd0, 0, 0)
                split_qk(hd0, 0, 1)
                split_wqk(hd0 + 2, 0, PAIRS * i + 1)
                with pool.If(i - B * (i // B) < 1):
                    for k in range(KT):
                        split_wp(i // B, k)
                split_qk(hd0 + 1, 1, 0)
                normalise(TILES * i, 0)
                normalise(TILES * i + 1, 1)
                v_low(hd0, 0, 0)
                with pool.Fori(0, PAIRS - 1) as p:
                    pair_steps(i, p, False)
                pair_steps(i, PAIRS - 1, True)

        @block.scalar
        def _(act):
            def evac_qk(hd, col, half, bank, before):
                if before:
                    act.wait_ge(qk_split, 2 * hd + half - 1)
                wait_alone(act, qk_acc, 2 * hd + half + 1)
                nc.scalar.activation(qk[:, half * HALF:(half + 1) * HALF], bank, ACT.Identity,
                                     bias=bqk_sc[:, bass.ds(col, 1)], scale=qk_scale[:, :]).then_inc(qk_evac, 1)

            def v_high(hd, hh, s, groups):
                if groups is not None:
                    act.wait_ge(pv_done, pv_at(groups - 1))
                nc.scalar.copy(v_st[s][:, :, 0:D], v_raw[:, :, bass.ds(hh * D, D)]).then_inc(v_hi_done, 1)

            def exponential(n, m, old):
                act.wait_ge(min_ready, n + 1)
                if old is not None:
                    act.wait_ge(transposed, old)
                nc.scalar.activation(probs[m % 2][:, :], ps_s[:, m % 2, :], ACT.Exp, bias=row_min[:, m % 4:m % 4 + 1],
                                     scale=-1.0, accum_out=row_sum[:, m % 4:m % 4 + 1]).then_inc(exp_ready, 1)

            def high_part(n, m, half):
                act.wait_ge(transposed, 2 * n + half + 1)
                nc.scalar.copy(pt_hi[:, m // 2 % 2, 4 * half:4 * half + 4, (m % 2) * P:(m % 2 + 1) * P],
                               ps_t[:, half, :].rearrange("p (b t) -> p b t", b=4)).then_inc(hi_ready, 1)

            def other_half(g, k):
                src, dst = (slice(D, P), slice(0, D)) if k < 4 else (slice(0, D), slice(D, P))
                act.wait_ge(pv_done, pv_at(g))
                nc.scalar.copy(o_part[k % 2][dst, :], ps_o[src, 0:GROUP]).then_inc(part_ready, 1)

            def x_high(seq, c):
                act.wait_ge(xn_f32, KT * seq + c + 1)
                nc.scalar.copy(xn_hi[:, c, :], x_raw[:, c, :]).then_inc(xn_hi_done, 1)

            def attn_high(pair, p, k):
                cols = slice(k * GROUP, (k + 1) * GROUP)
                act.wait_ge(attn_ready, sum_at(8 * pair + 4 + k))
                nc.scalar.copy(a_hi[:, bass.ds(p, 1), cols],
                               attn[:, cols].rearrange("p (o t) -> p o t", o=1)).then_inc(a_hi_done, 1)

            for c in range(KT):
                x_high(0, c)
            act.wait_ge(setup_done, 2)

            def pair_steps(i, p, last):
                pair = PAIRS * i + p
                tile = TILES * i + PT_STEPS * p
                col = (i // B) * H
                for e in range(2):
                    hh = 2 * p + e
                    hd = H * i + hh
                    for j in range(NT):
                        m = NT * e + j
                        if not last and m >= 4 and m % 2 == 0:
                            other_half(8 * pair + m // 2 - 2, m // 2 - 2)
                        high_part(tile + m, m, 0)
                        high_part(tile + m, m, 1)
                        if m == PT_STEPS - 1 or last and m >= 3 and m % 2 == 1:
                            other_half(8 * pair + (m - 3) // 2, (m - 3) // 2)
                        if not (last and m + 2 >= PT_STEPS):
                            exponential(tile + m + 2, m + 2, 2 * (tile + m) + 2)
                        if j in (3, 7) and not last:
                            evac_qk(hd + 2, col + hh + 2, j // 4, g_bank, True)
                        if j == 2 and not (last and e == 1):
                            v_high(hd + 1, hh + 1, 1 - e, 4 * hd)
                        if e == 1 and j in (4, 6):
                            attn_high(pair, p, (j - 4) // 2)
                attn_high(pair, p, 2)
                other_half(8 * pair + 7, 7)
                attn_high(pair, p, 3)
                if last:
                    for c in range(KT):
                        x_high(i + 1, c)

            with act.Fori(0, PASSES) as i:
                hd0 = H * i
                col = (i // B) * H
                evac_qk(hd0, col, 0, qk_bank[0][0], False)
                evac_qk(hd0, col, 1, qk_bank[0][1], False)
                evac_qk(hd0 + 1, col + 1, 0, qk_bank[1][0], True)
                evac_qk(hd0 + 1, col + 1, 1, qk_bank[1][1], True)
                act.wait_ge(out_stored, stored_before(i))
                exponential(TILES * i, 0, None)
                exponential(TILES * i + 1, 1, None)
                act.wait_ge(v_evac, 8 * i + 8)
                v_high(hd0, 0, 0, None)
                with act.Fori(0, PAIRS - 1) as p:
                    pair_steps(i, p, False)
                pair_steps(i, PAIRS - 1, True)

        @block.vector
        def _(dve):
            def smallest(n, m):
                dve.wait_ge(scores_ready, n + 1)
                nc.vector.tensor_reduce(row_min[:, m % 4:m % 4 + 1], ps_s[:, m % 2, :], AX.X, ALU.min).then_inc(min_ready, 1)

            def reciprocal(n, m):
                dve.wait_ge(exp_ready, n + 1)
                nc.vector.reciprocal(row_rcp[:, m % 4:m % 4 + 1], row_sum[:, m % 4:m % 4 + 1]).then_inc(rcp_ready, 1)

            def low_part(n, m, half):
                dve.wait_ge(hi_ready, 2 * n + half + 1)
                place = (slice(None), m // 2 % 2, slice(4 * half, 4 * half + 4), slice((m % 2) * P, (m % 2 + 1) * P))
                nc.vector.tensor_tensor(pt_lo[place], ps_t[:, half, :].rearrange("p (b t) -> p b t", b=4),
                                        f32(pt_hi[place]), ALU.subtract).then_inc(lo_ready, 1)

            def add_halves(pair, k):
                rows = slice(0, D) if k < 4 else slice(D, P)
                cols = slice((k % 4) * GROUP, (k % 4 + 1) * GROUP)
                dve.wait_ge(part_ready, 8 * pair + k + 1)
                if k < 4:
                    dve.wait_ge(a_ready, a_at(pair - 1, k))
                nc.vector.tensor_tensor(attn[rows, cols], ps_o[rows, 0:GROUP], o_part[k % 2][rows, :],
                                        ALU.add).then_inc(attn_ready, 1)

            def half_stats(seq, c):
                dve.wait_ge(x_loaded[c], 16 * (seq + 1))
                nc.vector.bn_stats(bn_part[:, c, 0:6], x_raw[:, c, 0:HALF])
                nc.vector.bn_stats(bn_part[:, c, 6:12], x_raw[:, c, HALF:T]).then_inc(half_stat_ready, 1)

            def channel_stats(seq, c):
                wait_alone(dve, half_stat_ready, KT * seq + c + 1)
                nc.vector.bn_aggr(bn[:, c, :], bn_part[:, c, :]).then_inc(stat_ready, 1)

            def link(ins, seq, k):
                ins.then_inc(chain, 1)
                dve.wait_ge(chain, CHAIN * seq + k)

            def group_spread(seq):
                dve.wait_ge(stat_sum, 2 * seq + 1)
                link(nc.vector.tensor_copy(gmean[:, :], stat_bank[:, 0:KT]), seq, 1)
                link(nc.vector.tensor_tensor(work[:, :], bn[:, :, 0], gmean[:, :], ALU.subtract), seq, 2)
                link(nc.vector.tensor_tensor(work[:, :], work[:, :], work[:, :], ALU.mult), seq, 3)
                link(nc.vector.tensor_tensor(spread[:, :], work[:, :], bn[:, :, 1], ALU.add), seq, 4)

            def norm_coefs(seq, lay):
                dve.wait_ge(stat_sum, 2 * seq + 2)
                link(nc.vector.tensor_scalar(var_eps[:, :], stat_bank[:, KT:2 * KT], EPS, None, ALU.add), seq, 5)
                link(nc.vector.tensor_scalar(neg_half[:, :], var_eps[:, :], -0.5, None, ALU.mult), seq, 6)
                link(nc.vector.tensor_scalar(seed[:, :], var_eps[:, :].bitcast(I32), 1, None,
                                             ALU.logical_shift_right), seq, 7)
                link(nc.vector.tensor_scalar(rstd_bits[:, :], seed[:, :], -1.0, float(RSQRT_SEED),
                                             ALU.mult, ALU.add), seq, 8)
                for it in range(3):
                    link(nc.vector.tensor_tensor(work[:, :], rstd, rstd, ALU.mult), seq, 9 + 3 * it)
                    link(nc.vector.tensor_tensor(work[:, :], work[:, :], neg_half[:, :], ALU.mult), seq, 10 + 3 * it)
                    link(nc.vector.scalar_tensor_tensor(out=rstd, in0=work[:, :], scalar=1.5, in1=rstd,
                                                        op0=ALU.add, op1=ALU.mult), seq, 11 + 3 * it)
                link(nc.vector.tensor_tensor(norm_a[:, :], rstd, nw_sb[:, bass.ds(lay * KT, KT)], ALU.mult), seq, 18)
                link(nc.vector.tensor_tensor(work[:, :], gmean[:, :], norm_a[:, :], ALU.mult), seq, 19)
                nc.vector.tensor_tensor(norm_b[:, :], nb_sb[:, bass.ds(lay * KT, KT)], work[:, :],
                                        ALU.subtract).then_inc(chain, 1)

            def x_low(seq, c):
                dve.wait_ge(xn_hi_done, KT * seq + c + 1)
                nc.vector.tensor_tensor(xn_lo[:, c, :], x_raw[:, c, :], f32(xn_hi[:, c, :]),
                                        ALU.subtract).then_inc(xn_ready, 1)

            def evac_v(i, lay, b):
                dve.wait_ge(v_acc, 8 * i + b + 1)
                nc.vector.tensor_tensor(v_raw[:, b, :].rearrange("p (o n) -> p o n", o=1),
                                        v_bank[b].rearrange("p (o n) -> p o n", o=1),
                                        bv_all[:, bass.ds(lay, 1), :], ALU.add).then_inc(v_evac, 1)

            def output(i, lay, q):
                o, cols = q // 2, slice((q % 2) * HALF, (q % 2 + 1) * HALF)
                dve.wait_ge(proj_acc, 8 * i + q + 1)
                dve.wait_ge(res_loaded_p if o < 2 else res_loaded, 32 * (i + 1))
                nc.vector.scalar_tensor_tensor(out=stage[o][:, cols], in0=out_bank[q],
                                               scalar=bo_sb[:, bass.ds(lay * KT + o, 1)], in1=stage[o][:, cols],
                                               op0=ALU.add, op1=ALU.add).then_inc(out_ready, 1)

            nc.vector.memset(scratch[:, 0:1], 0.0).then_inc(lo_ready, LO_CREDIT)
            nc.vector.memset(scratch[:, 1:2], 0.0).then_inc(attn_ready, SUM_CREDIT)
            nc.vector.memset(scratch[:, 2:3], 0.0).then_inc(out_ready, OUT_CREDIT)
            nc.vector.memset(scratch[:, 3:4], 0.0).then_inc(pv_done, PV_CREDIT)
            nc.vector.memset(qk_scale[0:D, :], -SCALE)
            nc.vector.memset(qk_scale[D:P, :], 1.0).then_inc(setup_done, 1)
            for c in range(KT):
                half_stats(0, c)
                if c > 0:
                    channel_stats(0, c - 1)
            channel_stats(0, KT - 1)
            group_spread(0)
            dve.wait_ge(const_loaded, 16 * 6)
            norm_coefs(0, 0)
            dve.wait_ge(setup_done, 1)
            nc.vector.tensor_scalar(bqk_sc[:, :], bqk_sb[:, :], qk_scale[:, :], None, ALU.mult).then_inc(setup_done, 1)
            for c in range(KT):
                x_low(0, c)

            def pair_steps(i, p, last):
                pair = PAIRS * i + p
                tile = TILES * i + PT_STEPS * p
                for m in range(PT_STEPS):
                    if not last and m >= 4 and m % 2 == 0:
                        add_halves(pair, m // 2 - 2)
                    if not (last and m + 2 >= PT_STEPS):
                        smallest(tile + m + 2, m + 2)
                    low_part(tile + m, m, 0)
                    low_part(tile + m, m, 1)
                    if m == PT_STEPS - 1 or last and m >= 3 and m % 2 == 1:
                        add_halves(pair, (m - 3) // 2)
                    if not (last and m + 2 >= PT_STEPS):
                        reciprocal(tile + m + 2, m + 2)
                    if last and m == PT_STEPS - 2:
                        half_stats(i + 1, 0)
                if last:
                    for c in range(1, KT):
                        half_stats(i + 1, c)
                        channel_stats(i + 1, c - 1)
                    channel_stats(i + 1, KT - 1)
                    group_spread(i + 1)
                add_halves(pair, 7)

            with dve.Fori(0, PASSES) as i:
                lay = i // B
                for b in range(4):
                    evac_v(i, lay, b)
                for m in range(2):
                    smallest(TILES * i + m, m)
                    evac_v(i, lay, 4 + 2 * m)
                    reciprocal(TILES * i + m, m)
                    evac_v(i, lay, 5 + 2 * m)
                with dve.Fori(0, PAIRS - 1) as p:
                    pair_steps(i, p, False)
                pair_steps(i, PAIRS - 1, True)
                norm_coefs(i + 1, within(next_pass(i) // B, 0, LAYERS - 1))
                for q in range(3):
                    output(i, lay, q)
                for c in range(KT):
                    x_low(i + 1, c)
                for q in range(3, 8):
                    output(i, lay, q)

        @block.tensor
        def _(pe):
            def mac(bank, stat, mov, n, first, last):
                hi_lo = ((0, 0), (0, 1), (1, 0))[n % 3]
                return nc.tensor.matmul(bank, stat[hi_lo[0]](n // 3), mov[hi_lo[1]](n // 3), start=first, stop=last)

            def qk_part(half, bank, s, lo, hi):
                stat = (lambda k: wqk_hi[s][:, k, :], lambda k: wqk_lo[s][:, k, :])
                mov = tuple((lambda k, xn=xn: xn[:, k, half * HALF:(half + 1) * HALF]) for xn in (xn_hi, xn_lo))
                for n in range(lo, hi):
                    mm = mac(bank, stat, mov, n, n == 0, n == 3 * KT - 1)
                if hi == 3 * KT:
                    mm.then_inc(qk_acc, 1)

            def values(b, lo=0, hi=3 * KT):
                stat = tuple((lambda k, xn=xn: xn[:, k, b * P:(b + 1) * P]) for xn in (xn_hi, xn_lo))
                mov = (lambda k: wv_hi[:, k, :], lambda k: wv_lo[:, k, :])
                for n in range(lo, hi):
                    mm = mac(v_bank[b], stat, mov, n, n == 0, n == 3 * KT - 1)
                if hi == 3 * KT:
                    mm.then_inc(v_acc, 1)

            def project(q, lo, hi):
                o, half = q // 2, q % 2
                stat = tuple((lambda k, w=w: w[:, k, o * P:(o + 1) * P]) for w in (wp_hi, wp_lo))
                mov = tuple((lambda k, a=a: a[:, k, half * HALF:(half + 1) * HALF]) for a in (a_hi, a_lo))
                for n in range(lo, hi):
                    mm = mac(out_bank[q], stat, mov, n, n == 0, n == 3 * KT - 1)
                if hi == 3 * KT:
                    mm.then_inc(proj_acc, 1)

            def scores(m, s):
                j = m % NT
                for half in range(2):
                    cols = slice(half * HALF, (half + 1) * HALF)
                    nc.tensor.matmul(ps_s[:, m % 2, cols], q_st[s][:, j * P:(j + 1) * P], kh_st[s][:, cols],
                                     start=True, stop=False)
                    mm = nc.tensor.matmul(ps_s[:, m % 2, cols], q_st[s][:, j * P:(j + 1) * P], kl_st[s][:, cols],
                                          start=False, stop=True)
                mm.then_inc(scores_ready, 1)

            def transpose(n, m):
                pe.wait_ge(probs_ready, n + 1)
                for half in range(2):
                    pe.wait_ge(lo_ready, lo_at(n - 1, half))
                    for b in range(4):
                        mm = nc.tensor.transpose(ps_t[:, half, b * P:(b + 1) * P],
                                                 probs[m % 2][:, (4 * half + b) * P:(4 * half + b + 1) * P], ident)
                    mm.then_inc(transposed, 1)

            def weigh(tile, g, hd, k, lo, hi):
                if lo == 0:
                    pe.wait_ge(attn_ready, sum_at(g - 1))
                    pe.wait_ge(v_ready, hd + 1)
                    pe.wait_ge(lo_ready, lo_at(tile + 2 * k + 1, 1))
                for b in range(lo, hi):
                    v = v_st[k // 4][:, b, :]
                    nc.tensor.matmul(ps_o[:, 0:GROUP], v, pt_hi[:, k % 2, b, :], start=(b == 0), stop=False)
                    mm = nc.tensor.matmul(ps_o[:, 0:GROUP], v, pt_lo[:, k % 2, b, :], start=False, stop=(b == BLK - 1))
                if hi == BLK:
                    mm.then_inc(pv_done, 1)

            def group_average(seq, what, cols):
                nc.tensor.matmul(stat_bank[:, cols], group_mean, what, start=True, stop=True).then_inc(stat_sum, 1)

            def average_means(seq):
                pe.wait_ge(stat_ready, KT * (seq + 1))
                group_average(seq, bn[:, :, 0], slice(0, KT))

            def average_spreads(seq):
                pe.wait_ge(chain, CHAIN * seq + 4)
                group_average(seq, spread[:, :], slice(KT, 2 * KT))

            pe.wait_ge(const_loaded, 16 * 6)
            average_means(0)
            average_spreads(0)

            def later_qk(i, m, hd, e, j):
                if m == 0:
                    pe.wait_ge(v_evac, 8 * i + 8)
                if j == 0:
                    pe.wait_ge(wqk_ready, hd + 3)
                if j % 4 == 0:
                    pe.wait_ge(qk_evac, 2 * (hd + 2) + j // 4)
                qk_part(j // 4, g_bank, e, LATER_QK[m], LATER_QK[m] + LATER_QK_N[m])

            def pair_steps(i, p, last):
                pair = PAIRS * i + p
                tile = TILES * i + PT_STEPS * p
                for e in range(2):
                    hh = 2 * p + e
                    hd = H * i + hh
                    for j in range(NT):
                        m = NT * e + j
                        if not (last and m + 2 >= PT_STEPS):
                            pe.wait_ge(exp_ready, tile + m + 1)
                            s = (m + 2) // NT % 2
                            if j == NT - 2:
                                pe.wait_ge(stacked[s], 32 * (4 * i + p + 1 + e))
                            scores(m + 2, s)
                        elif m == PT_STEPS - 2:
                            pe.wait_ge(exp_ready, tile + m + 1)
                            project(0, 0, 3)
                        else:
                            project(0, 3, 6)
                        transpose(tile + m, m)
                        if not last and m < PT_STEPS - 1:
                            later_qk(i, m, hd, e, j)
                        if last and m == 0:
                            pe.wait_ge(wp_ready, KT * (i // B + 1))
                            pe.wait_ge(qk_evac, 2 * H * (i + 1))
                            pe.wait_ge(a_ready, a_at(PAIRS * i + 1, 3))
                            project(6, 0, 6)
                        if last and m == 1:
                            pe.wait_ge(a_ready, a_at(PAIRS * i + 2, 3))
                            project(6, 6, 9)
                        if m >= 2:
                            k = (m - 2) // 2
                            weigh(tile, 8 * pair + k, H * i + 2 * p + k // 4, k, 4 * (m % 2), 4 * (m % 2) + 4)
                        if not last and m == PT_STEPS - 1:
                            later_qk(i, m, hd, e, j)

            with pe.Fori(0, PASSES) as i:
                hd0 = H * i
                pe.wait_ge(wqk_ready, hd0 + 1)
                for half in range(2):
                    pe.wait_ge(out_ready, out_at(i - 1, half))
                    for k in range(KT):
                        if half == 0:
                            pe.wait_ge(xn_ready, KT * i + k + 1)
                        qk_part(half, qk_bank[0][half], 0, 3 * k, 3 * k + 3)
                for b in range(4):
                    pe.wait_ge(out_ready, out_at(i - 1, 4 + b))
                    for k in range(KT):
                        if b == 0:
                            pe.wait_ge(wv_ready, KT * i + k + 1)
                        values(b, 3 * k, 3 * k + 3)
                pe.wait_ge(wqk_ready, hd0 + 2)
                for half in range(2):
                    qk_part(half, qk_bank[1][half], 1, 0, 3 * KT)
                pe.wait_ge(stacked[0], 32 * (4 * i + 1))
                scores(0, 0)
                for b in (4, 5):
                    pe.wait_ge(v_evac, 8 * i + b - 3)
                    values(b)
                pe.wait_ge(qk_evac, 2 * hd0 + 4)
                scores(1, 0)
                for b in (6, 7):
                    pe.wait_ge(v_evac, 8 * i + b - 3)
                    values(b)
                wait_alone(pe, v_evac, 8 * i + 6)
                with pe.Fori(0, PAIRS - 1) as p:
                    pair_steps(i, p, False)
                    pair = PAIRS * i + p
                    weigh(TILES * i + PT_STEPS * p, 8 * pair + 7, H * i + 2 * p + 1, 7, 0, BLK)
                pair_steps(i, PAIRS - 1, True)

                pe.wait_ge(exp_ready, TILES * (i + 1))
                project(0, 6, 9)
                for q in (1, 2):
                    project(q, 0, 9)
                weigh(TILES * i + PT_STEPS * (PAIRS - 1), GROUPS * (i + 1) - 1, H * i + H - 1, 7, 0, BLK)
                wait_alone(pe, lo_ready, lo_at(TILES * (i + 1) - 1, 1))
                average_means(i + 1)
                project(3, 0, 9)
                average_spreads(i + 1)
                project(4, 0, 9)
                pe.wait_ge(a_ready, a_at(PAIRS * i + 3, 3))
                for q in range(5):
                    project(q, 9, 12)
                pe.wait_ge(chain, CHAIN * (i + 2))
                project(5, 0, 12)
                project(6, 9, 12)
                project(7, 0, 12)


def kernel(**inputs):
    import concourse.bacc as bacc
    from concourse.bass_utils import run_bass_kernel_spmd

    def both(name0, name1):
        return np.stack([np.asarray(inputs["L0_conv_" + name0]), np.asarray(inputs["L1_conv_" + name1])])

    def columns(a):
        return np.ascontiguousarray(a.reshape(-1, P).T)

    qkv = both("qkv_w", "proj_w").reshape(LAYERS, H, 3, D, C)
    qkv_b = both("qkv_b", "proj_b").reshape(LAYERS, H, 3, D)
    proj = both("proj_w", "out_w")
    group = np.zeros((P, P), np.float32)
    per = C // NORM_GROUPS
    for g in range(P // per):
        group[g * per:(g + 1) * per, g * per:(g + 1) * per] = 1.0 / per
    wqk = qkv[:, :, 0:2].reshape(LAYERS * H, P, KT, P).transpose(0, 3, 2, 1)
    arrays = {
        "x": np.asarray(inputs["x"]).reshape(B, C, T),
        "wqk": wqk,
        "wv": qkv[:, :, 2].reshape(LAYERS, C, KT, P).transpose(0, 2, 3, 1),
        "wp": proj.reshape(LAYERS, C, KT, P).transpose(0, 2, 3, 1),
        "bqk": columns(qkv_b[:, :, 0:2].reshape(LAYERS, H * P)),
        "bv": qkv_b[:, :, 2].reshape(LAYERS, C),
        "bo": columns(both("proj_b", "out_b")),
        "nw": columns(both("norm_w", "norm_w")),
        "nb": columns(both("norm_b", "norm_b")),
        "consts": np.concatenate([np.eye(P, dtype=np.float32), group], axis=1),
    }
    arrays = {n: np.ascontiguousarray(a) for n, a in arrays.items()}
    nc = bacc.Bacc("TRN2", target_bir_lowering=False, num_devices=1)
    args = [nc.dram_tensor("in_" + n, a.shape, mybir.dt.from_np(a.dtype), kind="ExternalInput").ap()
            for n, a in arrays.items()]
    out = nc.dram_tensor("out", (B, C, T), F32, kind="ExternalOutput").ap()
    build(nc, *args, out)
    r = run_bass_kernel_spmd(nc, [{"in_" + n: a for n, a in arrays.items()}], core_ids=[0])
    return r.results[0]["out"].reshape(B, C, 32, 32)
```
